# Optimizing a Trainium2 kernel written in Bass

```python
import numpy as np
import jax
import jax.numpy as jnp

def _softmax(x, axis=-1):
    return jax.nn.softmax(x, axis=axis)

def _gelu(x):
    return jax.nn.gelu(x, approximate=True)

def _silu(x):
    return jax.nn.silu(x)

def _sigmoid(x):
    return jax.nn.sigmoid(x)

def _layernorm(x, axis=-1, eps=1e-05):
    m = jnp.mean(x, axis=axis, keepdims=True)
    v = jnp.var(x, axis=axis, keepdims=True)
    return (x - m) / jnp.sqrt(v + eps)

def _scatter_add(tgt, idx, src, axis=0):
    return tgt.at[idx].add(src)

def _segment_sum(src, seg, n):
    return jax.ops.segment_sum(src, seg, n)
kernel_name = 'mk_cond_resid_d2_seqx_r4_0b37c4'

def setup_inputs(seed: int=0):
    np.random.seed(seed)
    _w = jnp.asarray

    def _rec_inputs():
        import jax
        import jax.numpy as jnp
        _rk = jax.random.key(seed)
        x = -0.000125 + 0.9999 * jax.random.normal(jax.random.fold_in(_rk, 1), (8, 256, 256), jnp.float32)
        _lenS = 256 - jax.random.randint(jax.random.fold_in(_rk, 7), (8,), 0, max(1, 256 // 4) + 1, jnp.int32)
        _lenS2 = 256 - jax.random.randint(jax.random.fold_in(_rk, 8), (8,), 0, max(1, 256 // 4) + 1, jnp.int32)
        cond_1024 = 0.00513981 + 1.0024 * jax.random.normal(jax.random.fold_in(_rk, 11), (8, 256), jnp.float32)
        return (x, cond_1024)
    x, cond_1024 = _rec_inputs()

    def _L0_cond_setup():
        import jax, jax.numpy as jnp
        import numpy as np
        IN_FEATURES = 256
        OUT_FEATURES = 256
        BATCH = 32
        SEQ = 256
        EPS = 1e-08
        key = jax.random.key(seed)
        k1, k2, k3 = jax.random.split(key, 3)
        Efou = jax.random.normal(k1, (BATCH, SEQ, IN_FEATURES), dtype=jnp.float32)
        y = jax.random.normal(k2, (BATCH, IN_FEATURES), dtype=jnp.float32)
        weight = jax.random.normal(k3, (IN_FEATURES, OUT_FEATURES), dtype=jnp.float32)
        return {'Efou': Efou, 'y': y, 'weight': weight}
    _L0_cond_all = _L0_cond_setup()
    _L0_cond_in = {k: v for k, v in _L0_cond_all.items() if k in ('weight',)}
    del _L0_cond_all

    def _L1_cond_setup():
        import jax, jax.numpy as jnp
        import numpy as np
        B, T, C = (64, 128, 256)
        key = jax.random.key(seed)
        ks = jax.random.split(key, 17)
        s_in = 1.0 / np.sqrt(C)

        def lin(kw, kb, fan_in):
            s = 1.0 / np.sqrt(fan_in)
            W = jax.random.uniform(kw, (C, fan_in), jnp.float32, -s, s)
            b = jax.random.uniform(kb, (C,), jnp.float32, -s, s)
            return (W, b)
        Wxz, bxz = lin(ks[0], ks[1], C)
        Whz, bhz = lin(ks[2], ks[3], C)
        Wxr, bxr = lin(ks[4], ks[5], C)
        Whr, bhr = lin(ks[6], ks[7], C)
        Wxh, bxh = lin(ks[8], ks[9], C)
        Whh, bhh = lin(ks[10], ks[11], C)
        Whq, bhq = lin(ks[12], ks[13], C)
        X = jax.random.normal(ks[14], (B, T, C), jnp.float32)
        h0 = jax.random.normal(ks[15], (B, C), jnp.float32)
        return {'X': X, 'h0': h0, 'Wxz': Wxz, 'bxz': bxz, 'Whz': Whz, 'bhz': bhz, 'Wxr': Wxr, 'bxr': bxr, 'Whr': Whr, 'bhr': bhr, 'Wxh': Wxh, 'bxh': bxh, 'Whh': Whh, 'bhh': bhh, 'Whq': Whq, 'bhq': bhq}
    _L1_cond_all = _L1_cond_setup()
    _L1_cond_in = {k: v for k, v in _L1_cond_all.items() if k in ('Wxz', 'bxz', 'Whz', 'bhz', 'Wxr', 'bxr', 'Whr', 'bhr', 'Wxh', 'bxh', 'Whh', 'bhh', 'Whq', 'bhq')}
    del _L1_cond_all
    return {'x': x, 'cond_1024': cond_1024, 'L0_cond_weight': _L0_cond_in['weight'], 'L1_cond_Wxz': _L1_cond_in['Wxz'], 'L1_cond_bxz': _L1_cond_in['bxz'], 'L1_cond_Whz': _L1_cond_in['Whz'], 'L1_cond_bhz': _L1_cond_in['bhz'], 'L1_cond_Wxr': _L1_cond_in['Wxr'], 'L1_cond_bxr': _L1_cond_in['bxr'], 'L1_cond_Whr': _L1_cond_in['Whr'], 'L1_cond_bhr': _L1_cond_in['bhr'], 'L1_cond_Wxh': _L1_cond_in['Wxh'], 'L1_cond_bxh': _L1_cond_in['bxh'], 'L1_cond_Whh': _L1_cond_in['Whh'], 'L1_cond_bhh': _L1_cond_in['bhh'], 'L1_cond_Whq': _L1_cond_in['Whq'], 'L1_cond_bhq': _L1_cond_in['bhq']}

def reference(x, cond_1024, L0_cond_weight, L1_cond_Wxz, L1_cond_bxz, L1_cond_Whz, L1_cond_bhz, L1_cond_Wxr, L1_cond_bxr, L1_cond_Whr, L1_cond_bhr, L1_cond_Wxh, L1_cond_bxh, L1_cond_Whh, L1_cond_bhh, L1_cond_Whq, L1_cond_bhq):
    import jax
    import jax.numpy as jnp

    def _L0_cond_ref(Efou, y, weight):
        import jax, jax.numpy as jnp
        import numpy as np
        IN_FEATURES = 256
        OUT_FEATURES = 256
        BATCH = 32
        SEQ = 256
        EPS = 1e-08
        scale = 1.0 / np.sqrt(np.float32(weight.shape[0]))
        ys = y * scale
        d = jax.lax.rsqrt(jnp.einsum('bi,io->bo', ys * ys, weight * weight) + EPS)
        out = jnp.einsum('bsi,io->bso', Efou * ys[:, None, :], weight) * d[:, None, :]
        return out

    def _L1_cond_ref(X, h0, Wxz, bxz, Whz, bhz, Wxr, bxr, Whr, bhr, Wxh, bxh, Whh, bhh, Whq, bhq):
        import jax, jax.numpy as jnp
        import numpy as np
        B, T, C = (64, 128, 256)
        Xz = jnp.einsum('btc,hc->tbh', X, Wxz) + bxz
        Xr = jnp.einsum('btc,hc->tbh', X, Wxr) + bxr
        Xh = jnp.einsum('btc,hc->tbh', X, Wxh) + bxh

        def step(H, xs):
            xz, xr, xh = xs
            Z = jax.nn.sigmoid(xz + H @ Whz.T + bhz)
            R = jax.nn.sigmoid(xr + H @ Whr.T + bhr)
            H_tilda = jnp.tanh(xh + R * H @ Whh.T + bhh)
            H_new = Z * H + (1.0 - Z) * H_tilda
            Y = H_new @ Whq.T + bhq
            return (H_new, Y)
        _, Ys = jax.lax.scan(step, h0, (Xz, Xr, Xh))
        return jnp.transpose(Ys, (1, 0, 2))
    x = x + _L0_cond_ref(x, cond_1024, L0_cond_weight)
    x = x + _L1_cond_ref(x, cond_1024, L1_cond_Wxz, L1_cond_bxz, L1_cond_Whz, L1_cond_bhz, L1_cond_Wxr, L1_cond_bxr, L1_cond_Whr, L1_cond_bhr, L1_cond_Wxh, L1_cond_bxh, L1_cond_Whh, L1_cond_bhh, L1_cond_Whq, L1_cond_bhq)
    return x

_drawn_inputs = setup_inputs


def setup_inputs(seed=0):
    import zlib

    import numpy as np

    out = dict(_drawn_inputs(seed))
    spreads = {}
    factors = {'L1_cond_bxz': 25.497,
     'L1_cond_Whz': 3.857,
     'L1_cond_bhz': 27.414,
     'L1_cond_Wxr': 21.502,
     'L1_cond_bxr': 64.0,
     'L1_cond_Whr': 50.116,
     'L1_cond_bhr': 64.0,
     'L1_cond_bxh': 5.111,
     'L1_cond_bhh': 5.653}
    for name, (base, spread) in spreads.items():
        noise = np.random.default_rng([zlib.crc32(name.encode()), seed]).standard_normal(out[name].shape)
        drawn = base * np.exp(spread * noise) if base else spread * noise
        out[name] = jnp.asarray(drawn.astype(out[name].dtype))
    for name, factor in factors.items():
        out[name] = (out[name] * factor).astype(out[name].dtype)
    return out
```

```python
import concourse.bass as bass
from concourse import mybir
from contextlib import ExitStack


def modulated_linear_then_gru(
    nc: bass.Bass,
    x_cm: bass.AP,
    cond_cm: bass.AP,
    w_mod_cm: bass.AP,
    w_in_cm: bass.AP,
    w_rec_cm: bass.AP,
    w_out_cm: bass.AP,
    gate_bias: bass.AP,
    out_bias: bass.AP,
    out: bass.AP,
):
    fp32 = mybir.dt.float32
    bf16 = mybir.dt.bfloat16
    ALU = mybir.AluOpType
    ACT = mybir.ActivationFunctionType

    P = 128
    KC = x_cm.shape[1]
    C = P * KC
    B = cond_cm.shape[2]
    T = x_cm.shape[2] // B
    HALF = 8
    HC = HALF * B
    BLOCK = 2 * HALF
    ITERS = T // BLOCK
    R, Z, G = 0, 1, 2
    EPS = 1e-8
    SCALE = float(C) ** -0.5

    ctx = ExitStack()
    with ctx:
        def sb(name, shape, dt=fp32):
            return ctx.enter_context(nc.sbuf_tensor(name, shape, dt))

        def pb(name, shape):
            return ctx.enter_context(nc.psum_tensor(name, shape, fp32))

        def sem(name):
            return ctx.enter_context(nc.semaphore(name))

        x = sb("x", [P, KC, T * B])
        x1 = sb("x1", [P, KC, T * B])
        cond = sb("cond", [P, KC, B])
        w_mod = sb("w_mod", [P, KC, C])
        w_in = sb("w_in", [P, 3, KC, C])
        w_rec = sb("w_rec", [P, 3, KC, C])
        w_out = sb("w_out", [P, KC, C])
        bq = sb("bq", [P, KC])

        bias = sb("bias", [96, 3, C])
        bias_hi = sb("bias_hi", [96, 3, C], bf16)
        bias_rest = sb("bias_rest", [96, 3, C])
        bias_mid = sb("bias_mid", [96, 3, C], bf16)
        bias_rest2 = sb("bias_rest2", [96, 3, C])
        bias_parts = sb("bias_parts", [96, 3, C], bf16)
        ones = sb("ones", [96, HC], bf16)

        ys = sb("ys", [P, KC, B])
        ys_sq = sb("ys_sq", [P, KC, B])
        w_mod_sq = sb("w_mod_sq", [P, KC, C])
        d_sq = sb("d_sq", [P, KC, B])
        minus_half = sb("minus_half", [P, KC, B])
        d = sb("d", [P, KC, B])
        xs = sb("xs", [P, 2, KC, HALF, B])
        lin = sb("lin", [P, 2, KC, HALF, B])

        hidden = sb("hidden", [P, KC, BLOCK, B, 2])
        r_gate = sb("r_gate", [P, KC, B])
        z_gate = sb("z_gate", [P, KC, B])
        r_hidden = sb("r_hidden", [P, KC, B])
        scan_mul = sb("scan_mul", [P, KC, B, 2])
        scan_add = sb("scan_add", [P, KC, B, 2])
        result = sb("result", [P, KC, BLOCK * B])

        chunk_bank = [[pb(f"chunk_bank{p}{k}", [P, 512]) for k in range(KC)] for p in range(2)]
        z_bank = [pb(f"z_bank{p}", [P, 512]) for p in range(2)]
        y_bank = pb("y_bank", [P, 512])
        lin_bank = pb("lin_bank", [P, 512])

        def pre(parity, gate, m, lo, hi):
            if gate == Z:
                return z_bank[parity][:, m * HC + lo * B:m * HC + hi * B]
            at = 0 if gate == R else HC
            return chunk_bank[parity][m][:, at + lo * B:at + hi * B]

        ld_cond, ld_wmod, ld_bias, ld_bq = sem("ld_cond"), sem("ld_wmod"), sem("ld_bias"), sem("ld_bq")
        ld_x = [sem(f"ld_x{i}") for i in range(4)]
        ld_win, ld_wrec, ld_wout = sem("ld_win"), sem("ld_wrec"), sem("ld_wout")
        dve_step = sem("dve_step")
        wsq_ready = sem("wsq_ready")
        dsq_ready = sem("dsq_ready")
        d_sq_ready = sem("d_sq_ready")
        exponent_ready = sem("exponent_ready")
        d_ready = sem("d_ready")
        bias_ready = sem("bias_ready")
        ys_ready = sem("ys_ready")
        xs_ready = sem("xs_ready")
        linp_ready = sem("linp_ready")
        lin_ready = sem("lin_ready")
        x1_ready = sem("x1_ready")
        y_ready = sem("y_ready")
        res_ready = sem("res_ready")
        stored = sem("stored")
        pre_r = [sem(f"pre_r{k}") for k in range(KC)]
        pre_z = sem("pre_z")
        pre_g = [sem(f"pre_g{k}") for k in range(KC)]
        r_ready = [sem(f"r_ready{k}") for k in range(KC)]
        z_ready = sem("z_ready")
        g_ready = [sem(f"g_ready{k}") for k in range(KC)]
        rh_ready = [sem(f"rh_ready{k}") for k in range(KC)]
        gates_ready = sem("gates_ready")
        h_ready = [sem(f"h_ready{k}") for k in range(KC)]

        block = ctx.enter_context(nc.Block())

        @block.sync
        def _(sp):
            quarter = T * B // 4
            sp.dma_start(cond[:, :, :], cond_cm).then_inc(ld_cond, 16)
            sp.dma_start(x[:, :, 0:quarter], x_cm[:, :, 0:quarter]).then_inc(ld_x[0], 16)
            sp.dma_start(w_in[:, :, :, :], w_in_cm).then_inc(ld_win, 16)
            for i in range(1, 4):
                at = slice(i * quarter, (i + 1) * quarter)
                sp.dma_start(x[:, :, at], x_cm[:, :, at]).then_inc(ld_x[i], 16)

            sp.wait_ge(res_ready, KC)
            sp.dma_start(out[:, :, 0:HC], result[:, :, HC:2 * HC]).then_inc(stored, 16)
            with sp.Fori(1, ITERS) as it:
                sp.wait_ge(res_ready, it * (2 * KC) + KC)
                sp.dma_start(out[:, :, bass.ds(it * (2 * HC) - HC, 2 * HC)], result[:, :, :]).then_inc(stored, 16)
            sp.wait_ge(res_ready, ITERS * 2 * KC)
            sp.dma_start(out[:, :, T * B - HC:T * B], result[:, :, 0:HC]).then_inc(stored, 16)
            sp.wait_ge(stored, 16 * (ITERS + 1))

        @block.gpsimd
        def _(pool):
            def scale_x(n, parity):
                cols = bass.ds(n * HC, HC)
                for k in range(KC):
                    mul = nc.gpsimd.tensor_tensor(
                        xs[:, parity, k, :, :], x[:, k, cols].rearrange("p (t b) -> p t b", b=B),
                        ys[:, k, :].unsqueeze(1).to_broadcast([P, HALF, B]), ALU.mult)
                mul.then_inc(xs_ready, 1)

            def add_x(n, parity):
                cols = bass.ds(n * HC, HC)
                for k in range(KC):
                    add = nc.gpsimd.tensor_tensor(
                        x1[:, k, cols].rearrange("p (t b) -> p t b", b=B), lin[:, parity, k, :, :],
                        x[:, k, cols].rearrange("p (t b) -> p t b", b=B), ALU.add)
                add.then_inc(x1_ready, 1)

            nc.gpsimd.memset(minus_half[:, :, :], -0.5).then_inc(exponent_ready, 1)
            pool.wait_ge(exponent_ready, 1)
            pool.wait_ge(ys_ready, 1)
            pool.wait_ge(ld_x[0], 16)
            scale_x(0, 0)
            scale_x(1, 1)
            pool.wait_ge(d_sq_ready, 1)
            nc.gpsimd.tensor_tensor(d[:, :, :], d_sq[:, :, :], minus_half[:, :, :], ALU.pow).then_inc(d_ready, 1)
            for n in range(2):
                pool.wait_ge(lin_ready, n + 1)
                add_x(n, n)
            pool.wait_ge(linp_ready, 1)
            scale_x(2, 0)
            for i in range(1, 4):
                pool.wait_ge(ld_x[i], 16)

            def block_steps(it, last):
                for p in range(2):
                    n = it * 2 + p
                    if not (last and p == 1):
                        pool.wait_ge(linp_ready, n + 2)
                        scale_x(n + 3, (p + 1) % 2)
                    pool.wait_ge(lin_ready, n + 3)
                    add_x(n + 2, p)

            with pool.Fori(0, ITERS - 2) as it:
                block_steps(it, False)
            block_steps(ITERS - 2, True)

        @block.scalar
        def _(act):
            act.dma_start(w_mod[:, :, :], w_mod_cm).then_inc(ld_wmod, 16)
            act.dma_start(bias[:, :, :], gate_bias).then_inc(ld_bias, 16)
            act.dma_start(w_rec[:, :, :, :], w_rec_cm).then_inc(ld_wrec, 16)
            act.dma_start(w_out[:, :, :], w_out_cm).then_inc(ld_wout, 16)
            act.dma_start(bq[:, :], out_bias).then_inc(ld_bq, 16)

            def step(it, s):
                t = it * BLOCK + s
                p, j = s // HALF, s % HALF
                for k in range(KC):
                    act.wait_ge(pre_r[k], t + 1)
                    nc.scalar.activation(r_gate[:, k, :], pre(p, R, k, j, j + 1), ACT.Sigmoid).then_inc(r_ready[k], 1)
                act.wait_ge(pre_z, t + 1)
                zp = z_bank[p][:, 0:KC * HC].rearrange("p (k c) -> p k c", k=KC)[:, :, j * B:(j + 1) * B]
                nc.scalar.activation(z_gate[:, :, :], zp, ACT.Sigmoid).then_inc(z_ready, 1)
                for k in range(KC):
                    act.wait_ge(pre_g[k], t + 1)
                    nc.scalar.activation(scan_add[:, k, :, 0], pre(p, G, k, j, j + 1), ACT.Tanh).then_inc(g_ready[k], 1)

            with act.Fori(0, ITERS) as it:
                for s in range(BLOCK):
                    step(it, s)

        @block.vector
        def _(dve):
            done = [0]

            def own(ins):
                done[0] += 1
                ins.then_inc(dve_step, 1)
                dve.wait_ge(dve_step, done[0])

            dve.wait_ge(ld_cond, 16)
            own(nc.vector.tensor_scalar(ys[:, :, :], cond[:, :, :], SCALE, None, ALU.mult))
            nc.vector.tensor_copy(ys[:, :, :], ys[:, :, :]).then_inc(ys_ready, 1)
            dve.wait_ge(ys_ready, 1)
            own(nc.vector.tensor_tensor(ys_sq[:, :, :], ys[:, :, :], ys[:, :, :], ALU.mult))
            for k in range(KC):
                nc.vector.tensor_copy(hidden[:, k, BLOCK - 1, :, 1], cond[:, k, :]).then_inc(h_ready[k], 1)
            dve.wait_ge(ld_wmod, 16)
            nc.vector.tensor_tensor(w_mod_sq[:, :, :], w_mod[:, :, :], w_mod[:, :, :], ALU.mult).then_inc(wsq_ready, 1)
            nc.vector.memset(scan_mul[:, :, :, :], 0.0)
            own(nc.vector.memset(ones[:, :], 1.0))
            dve.wait_ge(dsq_ready, 1)
            sums = lin_bank[:, 0:KC * B].rearrange("p (k b) -> p k b", k=KC)
            nc.vector.tensor_scalar(d_sq[:, :, :], sums, EPS, None, ALU.add).then_inc(d_sq_ready, 1)

            dve.wait_ge(ld_bias, 16)
            own(nc.vector.tensor_copy(bias_hi[:, :, :], bias[:, :, :]))
            own(nc.vector.tensor_tensor(bias_rest[:, :, :], bias[:, :, :], bias_hi[:, :, :], ALU.subtract))
            own(nc.vector.tensor_copy(bias_mid[:, :, :], bias_rest[:, :, :]))
            own(nc.vector.tensor_tensor(bias_rest2[:, :, :], bias_rest[:, :, :], bias_mid[:, :, :], ALU.subtract))
            nc.vector.tensor_copy(bias_parts[0:32, :, :], bias_hi[0:32, :, :])
            nc.vector.tensor_copy(bias_parts[32:64, :, :], bias_mid[32:64, :, :])
            nc.vector.tensor_copy(bias_parts[64:96, :, :], bias_rest2[64:96, :, :]).then_inc(bias_ready, 1)

            def modulate(n, parity):
                prod = lin_bank[:, 0:KC * HC].rearrange("p (k t b) -> p k t b", k=KC, b=B)
                dve.wait_ge(linp_ready, n + 1)
                for k in range(KC):
                    mul = nc.vector.tensor_tensor(
                        lin[:, parity, k, :, :], prod[:, k, :, :],
                        d[:, k, :].unsqueeze(1).to_broadcast([P, HALF, B]), ALU.mult)
                mul.then_inc(lin_ready, 1)

            def finish(n, parity, k):
                at = HC * (1 - parity)
                nc.vector.scalar_tensor_tensor(
                    out=result[:, k, at:at + HC], in0=y_bank[:, k * HC:(k + 1) * HC], scalar=bq[:, k:k + 1],
                    in1=x1[:, k, bass.ds(n * HC, HC)], op0=ALU.add, op1=ALU.add).then_inc(res_ready, 1)

            dve.wait_ge(d_ready, 1)
            for n in range(2):
                modulate(n, n)
            dve.wait_ge(ld_bq, 16)

            def block_steps(it, first, last):
                for s in range(BLOCK):
                    t = it * BLOCK + s
                    p, j = s // HALF, s % HALF
                    n = it * 2 + p
                    before = (s - 1) % BLOCK
                    for k in range(KC):
                        dve.wait_ge(h_ready[k], t + 1)
                        dve.wait_ge(r_ready[k], t + 1)
                        nc.vector.tensor_tensor(r_hidden[:, k, :], r_gate[:, k, :], hidden[:, k, before, :, 1],
                                                ALU.mult).then_inc(rh_ready[k], 1)
                    if j == 3 and not (last):
                        modulate(n + 2, p)
                    if j in (4, 5) and not (first and p == 0):
                        if j == 4:
                            dve.wait_ge(y_ready, n)
                            if p == 0:
                                dve.wait_ge(stored, it * 16)
                            elif first:
                                pass
                        finish(n - 1, 1 - p, j - 4)
                    dve.wait_ge(z_ready, t + 1)
                    nc.vector.tensor_tensor(scan_add[:, :, :, 1], z_gate[:, :, :], hidden[:, :, before, :, 1],
                                            ALU.mult).then_inc(gates_ready, 1)
                    nc.vector.tensor_scalar(scan_mul[:, :, :, 1], z_gate[:, :, :], -1.0, 1.0, ALU.mult,
                                            ALU.add).then_inc(gates_ready, 1)
                    dve.wait_ge(gates_ready, 2 * t + 2)
                    for k in range(KC):
                        dve.wait_ge(g_ready[k], t + 1)
                        nc.vector.tensor_tensor_scan(
                            hidden[:, k, s, :, :].rearrange("p b two -> p (b two)"),
                            scan_mul[:, k, :, :].rearrange("p b two -> p (b two)"),
                            scan_add[:, k, :, :].rearrange("p b two -> p (b two)"),
                            0.0, ALU.mult, ALU.add).then_inc(h_ready[k], 1)

            block_steps(0, True, False)
            with dve.Fori(1, ITERS - 1) as it:
                block_steps(it, False, False)
            block_steps(ITERS - 1, False, True)
            dve.wait_ge(y_ready, 2 * ITERS)
            dve.wait_ge(stored, ITERS * 16)
            for k in range(KC):
                finish(2 * ITERS - 1, 1, k)

        @block.tensor
        def _(pe):
            def product(bank_cols, w, m, moving, first, last=True):
                for k in range(KC):
                    mm = nc.tensor.matmul(bank_cols, w[:, k, m * P:(m + 1) * P], moving(k),
                                          start=(first and k == 0), stop=True, skip_group_check=True)
                return mm

            def mod_product(parity, m):
                return product(lin_bank[:, m * HC:(m + 1) * HC], w_mod, m,
                               lambda k: xs[:, parity, k, :, :].rearrange("p t b -> p (t b)"), m == 0)

            def in_product(n, parity, gate, m):
                cols = pre(parity, gate, m, 0, HALF)
                first = (gate == R) or (gate == Z and m == 0)
                product(cols, w_in[:, gate, :, :], m, lambda k: x1[:, k, bass.ds(n * HC, HC)], first)
                return nc.tensor.matmul(cols, bias_parts[:, gate, m * P:(m + 1) * P], ones[:, :],
                                        start=False, stop=True, skip_group_check=True)

            def out_product(parity, m):
                return product(y_bank[:, m * HC:(m + 1) * HC], w_out, m,
                               lambda k: hidden[:, k, parity * HALF:(parity + 1) * HALF, :, 1]
                               .rearrange("p t b -> p (t b)"), m == 0)

            def rec_tile(parity, gate, m, k, j, moving):
                return nc.tensor.matmul(pre(parity, gate, m, j, j + 1), w_rec[:, gate, k, m * P:(m + 1) * P], moving,
                                        start=False, stop=True, skip_group_check=True)

            pe.wait_ge(wsq_ready, 1)
            for m in range(KC):
                mm = product(lin_bank[:, m * B:(m + 1) * B], w_mod_sq, m, lambda k: ys_sq[:, k, :], m == 0)
            mm.then_inc(dsq_ready, 1)
            pe.wait_ge(d_sq_ready, 1)
            for n in range(2):
                pe.wait_ge(xs_ready, n + 1)
                if n:
                    pe.wait_ge(lin_ready, n)
                for m in range(KC):
                    mm = mod_product(n, m)
                mm.then_inc(linp_ready, 1)
            pe.wait_ge(ld_win, 16)
            pe.wait_ge(bias_ready, 1)
            pe.wait_ge(x1_ready, 1)
            for gate in (R, Z, G):
                for m in range(KC):
                    in_product(0, 0, gate, m)
            pe.wait_ge(ld_wrec, 16)
            pe.wait_ge(ld_wout, 16)

            def block_steps(it, first, last):
                for s in range(BLOCK):
                    t = it * BLOCK + s
                    p, j = s // HALF, s % HALF
                    n = it * 2 + p
                    before = (s - 1) % BLOCK

                    pe.wait_ge(h_ready[0], t + 1)
                    rec_tile(p, R, 0, 0, j, hidden[:, 0, before, :, 1])
                    if not (first and s == 0):
                        pe.wait_ge(g_ready[1], t)
                    rec_tile(p, R, 1, 0, j, hidden[:, 0, before, :, 1])
                    pe.wait_ge(h_ready[1], t + 1)
                    rec_tile(p, R, 0, 1, j, hidden[:, 1, before, :, 1]).then_inc(pre_r[0], 1)
                    rec_tile(p, R, 1, 1, j, hidden[:, 1, before, :, 1]).then_inc(pre_r[1], 1)

                    for k in range(KC):
                        for m in range(KC):
                            mm = rec_tile(p, Z, m, k, j, hidden[:, k, before, :, 1])
                    mm.then_inc(pre_z, 1)

                    pe.wait_ge(rh_ready[0], t + 1)
                    rec_tile(p, G, 0, 0, j, r_hidden[:, 0, :])
                    pe.wait_ge(r_ready[1], t + 1)
                    rec_tile(p, G, 1, 0, j, r_hidden[:, 0, :])
                    pe.wait_ge(rh_ready[1], t + 1)
                    rec_tile(p, G, 0, 1, j, r_hidden[:, 1, :]).then_inc(pre_g[0], 1)
                    rec_tile(p, G, 1, 1, j, r_hidden[:, 1, :]).then_inc(pre_g[1], 1)

                    if j < 2:
                        if not last:
                            if j == 0:
                                pe.wait_ge(xs_ready, n + 3)
                                pe.wait_ge(lin_ready, n + 2)
                            mm = mod_product(p, j)
                            if j == 1:
                                mm.then_inc(linp_ready, 1)
                    elif not (last and p == 1):
                        if j == 2:
                            pe.wait_ge(x1_ready, n + 2)
                        gate, m = ((R, 0), (R, 1), (Z, 0), (Z, 1), (G, 0), (G, 1))[j - 2]
                        in_product(n + 1, 1 - p, gate, m)
                    if j in (0, 1) and not (first and p == 0):
                        if j == 0 and not (first and p == 1):
                            pe.wait_ge(res_ready, KC * (n - 1))
                        mm = out_product(1 - p, j)
                        if j == 1:
                            mm.then_inc(y_ready, 1)

            block_steps(0, True, False)
            with pe.Fori(1, ITERS - 1) as it:
                block_steps(it, False, False)
            block_steps(ITERS - 1, False, True)
            for k in range(KC):
                pe.wait_ge(h_ready[k], T + 1)
            pe.wait_ge(res_ready, KC * (2 * ITERS - 1))
            for m in range(KC):
                mm = out_product(1, m)
            mm.then_inc(y_ready, 1)


def kernel(**inputs):
    import numpy as np
    import concourse.bacc as bacc
    from concourse.bass_utils import run_bass_kernel_spmd

    def channel_major(a):
        return np.ascontiguousarray(np.asarray(a).T.reshape(-1, 128, a.shape[0]).transpose(1, 0, 2))

    x = np.asarray(inputs["x"])
    nb, nt, nch = x.shape
    w = {g: (inputs[f"L1_cond_Wx{g}"], inputs[f"L1_cond_Wh{g}"]) for g in "rzh"}
    bias = np.zeros((96, 3, nch), x.dtype)
    for i, g in enumerate("rzh"):
        for row in (0, 32, 64):
            bias[row, i] = inputs[f"L1_cond_bx{g}"]
            bias[row + 1, i] = inputs[f"L1_cond_bh{g}"]
    arrays = {
        "x_cm": channel_major(x.transpose(1, 0, 2).reshape(nt * nb, nch)),
        "cond_cm": channel_major(inputs["cond_1024"]),
        "w_mod_cm": channel_major(np.asarray(inputs["L0_cond_weight"]).T),
        "w_in_cm": np.ascontiguousarray(np.stack([channel_major(w[g][0]) for g in "rzh"], 1)),
        "w_rec_cm": np.ascontiguousarray(np.stack([channel_major(w[g][1]) for g in "rzh"], 1)),
        "w_out_cm": channel_major(inputs["L1_cond_Whq"]),
        "gate_bias": bias,
        "out_bias": np.ascontiguousarray(np.asarray(inputs["L1_cond_bhq"]).reshape(-1, 128).T),
    }
    nc = bacc.Bacc("TRN2", target_bir_lowering=False, num_devices=1)
    args = [nc.dram_tensor(k, a.shape, mybir.dt.from_np(a.dtype), kind="ExternalInput").ap() for k, a in arrays.items()]
    out = nc.dram_tensor("out_cm", (128, nch // 128, nt * nb), mybir.dt.from_np(x.dtype), kind="ExternalOutput").ap()
    modulated_linear_then_gru(nc, *args, out)
    got = run_bass_kernel_spmd(nc, [arrays], core_ids=[0]).results[0]["out_cm"]
    return np.ascontiguousarray(got.reshape(128, nch // 128, nt, nb).transpose(3, 2, 1, 0).reshape(nb, nt, nch))
```

```python
import concourse.bass as bass
from concourse import mybir
from contextlib import ExitStack


def modulated_linear_then_gru(
    nc: bass.Bass,
    x_cm: bass.AP,
    cond_cm: bass.AP,
    w_mod_cm: bass.AP,
    w_in_cm: bass.AP,
    w_rec_cm: bass.AP,
    w_out_cm: bass.AP,
    gate_bias: bass.AP,
    out_bias: bass.AP,
    out: bass.AP,
):
    fp32 = mybir.dt.float32
    bf16 = mybir.dt.bfloat16
    ALU = mybir.AluOpType
    ACT = mybir.ActivationFunctionType

    P = 128
    KC = x_cm.shape[1]
    C = P * KC
    B = cond_cm.shape[2]
    T = x_cm.shape[2] // B
    BLOCK = 16
    BC = BLOCK * B
    BODY = 2 * BLOCK
    ITERS = T // BODY
    NB = T // BLOCK
    GROUPS = 4
    GC = T * B // GROUPS
    PARTS = 3
    R, Z, G = 0, 1, 2
    EPS = 1e-8
    SCALE = float(C) ** -0.5

    ctx = ExitStack()
    with ctx:
        def sb(name, shape, dt=fp32):
            return ctx.enter_context(nc.sbuf_tensor(name, shape, dt))

        def pb(name):
            return ctx.enter_context(nc.psum_tensor(name, [P, 512], fp32))

        def sem(name):
            return ctx.enter_context(nc.semaphore(name))

        x = sb("x", [P, KC, T * B])
        x1 = sb("x1", [P, KC, (1 + NB + 1) * BC])
        cond = sb("cond", [P, KC, B])
        w_mod = sb("w_mod", [P, KC, C])
        w_in = sb("w_in", [P, 3, KC, C])
        w_rec = sb("w_rec", [P, 3, KC, C])
        w_rest = sb("w_rest", [P, 3, KC, C])
        w_part = [sb(f"w_part{i}", [P, 3, KC, C], bf16) for i in range(PARTS)]
        w_out = sb("w_out", [P, KC, C])
        bq = sb("bq", [P, KC])

        bias = sb("bias", [96, 3, C])
        bias_hi = sb("bias_hi", [96, 3, C], bf16)
        bias_rest = sb("bias_rest", [96, 3, C])
        bias_mid = sb("bias_mid", [96, 3, C], bf16)
        bias_rest2 = sb("bias_rest2", [96, 3, C])
        bias_parts = sb("bias_parts", [96, 3, C], bf16)
        ones = sb("ones", [96, BC], bf16)

        ys = sb("ys", [P, KC, B])
        ys_sq = sb("ys_sq", [P, KC, B])
        w_mod_sq = sb("w_mod_sq", [P, KC, C])
        d_sq = sb("d_sq", [P, KC, B])
        minus_half = sb("minus_half", [P, KC, B])
        d = sb("d", [P, KC, B])
        xs = sb("xs", [P, KC, T, B])
        lin = sb("lin", [P, KC, T, B])

        PART = 3 * B
        hidden = sb("hidden", [P, KC, BODY, PARTS * PART])
        r_hidden = sb("r_hidden", [P, KC, PARTS, B])
        r_gate = sb("r_gate", [P, KC, B])
        z_sum = sb("z_sum", [P, KC, B])
        z_pre = sb("z_pre", [P, KC, B])
        scan_mul = sb("scan_mul", [P, KC, PART])
        result = sb("result", [P, 2, KC, BC])

        hidden_bf = hidden[:, :, :, :].bitcast(bf16)
        r_hidden_bf = r_hidden[:, :, :, :].rearrange("p k g b -> p k (g b)").bitcast(bf16)
        every_chunk = slice(0, KC)

        def h_word(k, slot, part=0):
            return hidden[:, k, slot, PART * part + 2:PART * (part + 1):3]

        def h_parts(k, slot, lo, hi):
            return hidden_bf[:, k, slot, 2 * PART * lo + 5:2 * PART * hi:6]

        def rh_parts(k, lo, hi):
            return r_hidden_bf[:, k, 2 * B * lo + 1:2 * B * hi:2]

        chunk_bank = [[pb(f"chunk_bank{p}{k}") for k in range(KC)] for p in range(2)]
        z_bank = [pb(f"z_bank{p}") for p in range(2)]
        z_rec_bank = pb("z_rec_bank")
        y_bank = pb("y_bank")
        lin_bank = [chunk_bank[1], [z_bank[1], y_bank]]

        def pre(parity, gate, m, lo, hi):
            if gate == Z:
                return z_bank[parity][:, m * BC + lo * B:m * BC + hi * B]
            at = 0 if gate == R else BC
            return chunk_bank[parity][m][:, at + lo * B:at + hi * B]

        ld_cond, ld_wmod, ld_bias, ld_bq = sem("ld_cond"), sem("ld_wmod"), sem("ld_bias"), sem("ld_bq")
        ld_x = [sem(f"ld_x{i}") for i in range(GROUPS)]
        ld_win, ld_wrec, ld_wout = sem("ld_win"), sem("ld_wrec"), sem("ld_wout")
        dve_step = sem("dve_step")
        ys_ready = sem("ys_ready")
        wsq_ready = sem("wsq_ready")
        dsq_ready = sem("dsq_ready")
        d_sq_ready = sem("d_sq_ready")
        exponent_ready = sem("exponent_ready")
        d_ready = sem("d_ready")
        bias_ready = sem("bias_ready")
        part_ready = sem("part_ready")
        rest_ready = sem("rest_ready")
        xs_ready = sem("xs_ready")
        linp_ready = sem("linp_ready")
        lin_ready = sem("lin_ready")
        x1_ready = sem("x1_ready")
        y_ready = sem("y_ready")
        res_ready = sem("res_ready")
        stored = [sem(f"stored{q}") for q in range(2)]
        pre_r = [sem(f"pre_r{k}") for k in range(KC)]
        rec_z = sem("rec_z")
        pre_g = [sem(f"pre_g{k}") for k in range(KC)]
        r_ready = [sem(f"r_ready{k}") for k in range(KC)]
        g_ready = [sem(f"g_ready{k}") for k in range(KC)]
        rh_ready = [sem(f"rh_ready{k}") for k in range(KC)]
        rh_rest = sem("rh_rest")
        rh_rest2 = sem("rh_rest2")
        z_summed = sem("z_summed")
        pre_z = sem("pre_z")
        h_ready = [sem(f"h_ready{k}") for k in range(KC)]
        h_rest = [sem(f"h_rest{k}") for k in range(KC)]
        h_rest2 = sem("h_rest2")

        block = ctx.enter_context(nc.Block())

        @block.sync
        def _(sp):
            sp.dma_start(cond[:, :, :], cond_cm).then_inc(ld_cond, 16)
            for q in range(2):
                sp.sem_inc(stored[q], 16)
            sp.dma_start(x[:, :, 0:GC], x_cm[:, :, 0:GC]).then_inc(ld_x[0], 16)
            sp.dma_start(w_rec[:, :, :, :], w_rec_cm).then_inc(ld_wrec, 16)
            for i in range(1, GROUPS):
                at = slice(i * GC, (i + 1) * GC)
                sp.dma_start(x[:, :, at], x_cm[:, :, at]).then_inc(ld_x[i], 16)
            sp.dma_start(w_out[:, :, :], w_out_cm).then_inc(ld_wout, 16)

            def store(n, parity):
                sp.wait_ge(res_ready, (n + 1) * KC)
                sp.dma_start(out[:, :, bass.ds(n * BC, BC)], result[:, 1 - parity, :, :]
                             ).then_inc(stored[1 - parity], 16)

            with sp.Fori(0, ITERS) as it:
                for p in range(2):
                    store(it * 2 + p, p)
            store(NB, 0)
            sp.wait_ge(stored[0], 16 + 16 * ITERS)
            sp.wait_ge(stored[1], 16 + 16 * (ITERS + 1))

        @block.gpsimd
        def _(pool):
            nc.gpsimd.memset(minus_half[:, :, :], -0.5).then_inc(exponent_ready, 1)
            nc.gpsimd.memset(x1[:, :, 0:BC], 0.0)
            nc.gpsimd.memset(x1[:, :, (1 + NB) * BC:], 0.0).then_inc(x1_ready, 1)
            pool.wait_ge(exponent_ready, 1)
            pool.wait_ge(d_sq_ready, 1)
            nc.gpsimd.tensor_tensor(d[:, :, :], d_sq[:, :, :], minus_half[:, :, :], ALU.pow).then_inc(d_ready, 1)
            for i in range(GROUPS):
                pool.wait_ge(lin_ready, i + 1)
                for k in range(KC):
                    add = nc.gpsimd.tensor_tensor(
                        x1[:, k, BC + i * GC:BC + (i + 1) * GC],
                        lin[:, k, :, :].rearrange("p t b -> p (t b)")[:, i * GC:(i + 1) * GC],
                        x[:, k, i * GC:(i + 1) * GC], ALU.add)
                add.then_inc(x1_ready, 1)

        @block.scalar
        def _(act):
            act.dma_start(w_mod[:, :, :], w_mod_cm).then_inc(ld_wmod, 16)
            act.dma_start(bias[:, :, :], gate_bias).then_inc(ld_bias, 16)
            act.dma_start(w_in[:, :, :, :], w_in_cm).then_inc(ld_win, 16)
            act.dma_start(bq[:, :], out_bias).then_inc(ld_bq, 16)
            act.wait_ge(ld_wrec, 16)
            nc.scalar.activation(w_part[0][:, :, :, :], w_rec[:, :, :, :], ACT.Copy).then_inc(part_ready, 1)
            act.wait_ge(rest_ready, 1)
            nc.scalar.activation(w_part[1][:, :, :, :], w_rest[:, :, :, :], ACT.Copy).then_inc(part_ready, 1)

            with act.Fori(0, ITERS) as it:
                for s in range(BODY):
                    t = it * BODY + s
                    p, j = s // BLOCK, s % BLOCK
                    for k in range(KC):
                        act.wait_ge(pre_r[k], t + 1)
                        nc.scalar.activation(r_gate[:, k, :], pre(p, R, k, j, j + 1),
                                             ACT.Sigmoid).then_inc(r_ready[k], 1)
                    act.wait_ge(pre_z, t + 1)
                    nc.scalar.activation(scan_mul[:, :, 2::3], z_pre[:, :, :], ACT.Sigmoid, scale=-1.0)
                    for k in range(KC):
                        act.wait_ge(pre_g[k], t + 1)
                        nc.scalar.activation(hidden[:, k, (s - 1) % BODY, 3:3 + PART:3], pre(p, G, k, j, j + 1),
                                             ACT.Tanh).then_inc(g_ready[k], 1)

        @block.vector
        def _(dve):
            done = [0]

            def own(ins):
                done[0] += 1
                ins.then_inc(dve_step, 1)
                dve.wait_ge(dve_step, done[0])

            def split_h(slot, t1):
                for k in range(KC):
                    dve.wait_ge(h_ready[k], t1)
                    nc.vector.tensor_tensor(h_word(k, slot, 1), h_word(k, slot), h_parts(k, slot, 0, 1), ALU.subtract
                                            ).then_inc(h_rest[k], 1)
                dve.wait_ge(h_rest[1], t1)
                nc.vector.tensor_tensor(h_word(every_chunk, slot, 2), h_word(every_chunk, slot, 1),
                                        h_parts(every_chunk, slot, 1, 2), ALU.subtract).then_inc(h_rest2, 1)
                nc.vector.tensor_copy(hidden[:, :, slot, 4:4 + PART:3], h_word(every_chunk, slot))

            dve.wait_ge(ld_cond, 16)
            own(nc.vector.tensor_scalar(ys[:, :, :], cond[:, :, :], SCALE, None, ALU.mult))
            nc.vector.tensor_tensor(ys_sq[:, :, :], ys[:, :, :], ys[:, :, :], ALU.mult).then_inc(ys_ready, 1)
            dve.wait_ge(ld_wmod, 16)
            nc.vector.tensor_tensor(w_mod_sq[:, :, :], w_mod[:, :, :], w_mod[:, :, :], ALU.mult).then_inc(wsq_ready, 1)

            def scale_x(i):
                dve.wait_ge(ld_x[i], 16)
                steps = slice(i * T // GROUPS, (i + 1) * T // GROUPS)
                for k in range(KC):
                    mul = nc.vector.tensor_tensor(
                        xs[:, k, steps, :], x[:, k, i * GC:(i + 1) * GC].rearrange("p (t b) -> p t b", b=B),
                        ys[:, k, :].unsqueeze(1).to_broadcast([P, T // GROUPS, B]), ALU.mult)
                mul.then_inc(xs_ready, 1)

            def modulate(i):
                dve.wait_ge(linp_ready, i + 1)
                steps = slice(i * T // GROUPS, (i + 1) * T // GROUPS)
                for k in range(KC):
                    mul = nc.vector.tensor_tensor(
                        lin[:, k, steps, :], lin_bank[i % 2][k][:, :].rearrange("p (t b) -> p t b", b=B),
                        d[:, k, :].unsqueeze(1).to_broadcast([P, T // GROUPS, B]), ALU.mult)
                mul.then_inc(lin_ready, 1)

            scale_x(0)
            own(nc.vector.memset(hidden[:, :, :, :], 0.0))
            for k in range(KC):
                nc.vector.tensor_copy(h_word(k, BODY - 1), cond[:, k, :]).then_inc(h_ready[k], 1)
            dve.wait_ge(dsq_ready, 1)
            nc.vector.tensor_scalar(d_sq[:, :, :], z_rec_bank[:, 0:KC * B].rearrange("p (k b) -> p k b", k=KC),
                                    EPS, None, ALU.add).then_inc(d_sq_ready, 1)
            split_h(BODY - 1, 1)
            own(nc.vector.memset(scan_mul[:, :, :], 0.0))
            own(nc.vector.memset(scan_mul[:, :, 1::3], -1.0))
            own(nc.vector.memset(ones[:, :], 1.0))
            for i in range(1, GROUPS):
                scale_x(i)
                if i == 1:
                    dve.wait_ge(d_ready, 1)
                modulate(i - 1)
                if i == 1:
                    dve.wait_ge(ld_bias, 16)
                    own(nc.vector.tensor_copy(bias_hi[:, :, :], bias[:, :, :]))
                    own(nc.vector.tensor_tensor(bias_rest[:, :, :], bias[:, :, :], bias_hi[:, :, :], ALU.subtract))
                    own(nc.vector.tensor_copy(bias_mid[:, :, :], bias_rest[:, :, :]))
                    own(nc.vector.tensor_tensor(bias_rest2[:, :, :], bias_rest[:, :, :], bias_mid[:, :, :],
                                                ALU.subtract))
                    nc.vector.tensor_copy(bias_parts[0:32, :, :], bias_hi[0:32, :, :])
                    nc.vector.tensor_copy(bias_parts[32:64, :, :], bias_mid[32:64, :, :])
                    nc.vector.tensor_copy(bias_parts[64:96, :, :], bias_rest2[64:96, :, :]).then_inc(bias_ready, 1)
                if i == 2:
                    dve.wait_ge(part_ready, 1)
                    nc.vector.tensor_tensor(w_rest[:, :, :, :], w_rec[:, :, :, :], w_part[0][:, :, :, :],
                                            ALU.subtract).then_inc(rest_ready, 1)
            modulate(GROUPS - 1)
            dve.wait_ge(part_ready, 2)
            nc.vector.tensor_tensor(w_part[2][:, :, :, :], w_rest[:, :, :, :], w_part[1][:, :, :, :],
                                    ALU.subtract).then_inc(rest_ready, 1)
            dve.wait_ge(ld_bq, 16)

            def finish(it, n, parity, k):
                if k == 0:
                    dve.wait_ge(stored[1 - parity], it * 16 + 16)
                nc.vector.scalar_tensor_tensor(
                    out=result[:, 1 - parity, k, :], in0=y_bank[:, k * BC:(k + 1) * BC], scalar=bq[:, k:k + 1],
                    in1=x1[:, k, bass.ds(n * BC, BC)], op0=ALU.add, op1=ALU.add).then_inc(res_ready, 1)

            with dve.Fori(0, ITERS) as it:
                for s in range(BODY):
                    t = it * BODY + s
                    p, j = s // BLOCK, s % BLOCK
                    n = it * 2 + p
                    before = (s - 1) % BODY
                    for k in range(KC):
                        dve.wait_ge(r_ready[k], t + 1)
                        nc.vector.tensor_tensor(r_hidden[:, k, 0, :], r_gate[:, k, :], h_word(k, before),
                                                ALU.mult).then_inc(rh_ready[k], 1)
                    dve.wait_ge(rh_ready[1], t + 1)
                    nc.vector.tensor_tensor(r_hidden[:, :, 1, :], r_hidden[:, :, 0, :],
                                            r_hidden_bf[:, :, 1:2 * B:2], ALU.subtract).then_inc(rh_rest, 1)
                    dve.wait_ge(rec_z, t + 1)
                    nc.vector.tensor_reduce(
                        z_sum[:, :, :],
                        z_rec_bank[:, 0:KC * PARTS * B].rearrange("p (m g b) -> p m b g", m=KC, g=PARTS),
                        axis=mybir.AxisListType.X, op=ALU.add).then_inc(z_summed, 1)
                    dve.wait_ge(rh_rest, t + 1)
                    nc.vector.tensor_tensor(r_hidden[:, :, 2, :], r_hidden[:, :, 1, :],
                                            r_hidden_bf[:, :, 2 * B + 1:4 * B:2], ALU.subtract).then_inc(rh_rest2, 1)
                    dve.wait_ge(z_summed, t + 1)
                    nc.vector.tensor_tensor(
                        z_pre[:, :, :], z_sum[:, :, :],
                        z_bank[p][:, 0:KC * BC].rearrange("p (m c) -> p m c", m=KC)[:, :, j * B:(j + 1) * B],
                        ALU.add).then_inc(pre_z, 1)
                    if j in (8, 9):
                        if j == 8:
                            dve.wait_ge(y_ready, n + 1)
                        finish(it, n, p, j - 8)
                    for k in range(KC):
                        dve.wait_ge(g_ready[k], t + 1)
                        nc.vector.tensor_tensor_scan(hidden[:, k, s, 0:PART], scan_mul[:, k, :],
                                                     hidden[:, k, before, 2:2 + PART], 0.0, ALU.mult, ALU.add
                                                     ).then_inc(h_ready[k], 1)
                    split_h(s, t + 2)

            dve.wait_ge(y_ready, NB + 1)
            for k in range(KC):
                finish(ITERS, NB, 0, k)

        @block.tensor
        def _(pe):
            def product(cols, w, m, moving, first):
                for k in range(KC):
                    mm = nc.tensor.matmul(cols, w[:, k, m * P:(m + 1) * P], moving(k),
                                          start=(first and k == 0), stop=True, skip_group_check=True)
                return mm

            def in_tile(n, parity, gate, m, k):
                first = k == 0 and (gate == R or (gate == Z and m == 0))
                return nc.tensor.matmul(pre(parity, gate, m, 0, BLOCK), w_in[:, gate, k, m * P:(m + 1) * P],
                                        x1[:, k, bass.ds((n + 1) * BC, BC)],
                                        start=first, stop=True, skip_group_check=True)

            def in_bias(parity, gate, m):
                return nc.tensor.matmul(pre(parity, gate, m, 0, BLOCK), bias_parts[:, gate, m * P:(m + 1) * P],
                                        ones[:, :], start=False, stop=True, skip_group_check=True)

            def out_tile(parity, m, k):
                return nc.tensor.matmul(y_bank[:, m * BC:(m + 1) * BC], w_out[:, k, m * P:(m + 1) * P],
                                        h_word(k, slice(parity * BLOCK, (parity + 1) * BLOCK)),
                                        start=(m == 0 and k == 0), stop=True, skip_group_check=True)

            def rec(cols, gate, m, k, wp, moving, first=False):
                return nc.tensor.matmul(cols, w_part[wp][:, gate, k, m * P:(m + 1) * P], moving,
                                        start=first, stop=True, skip_group_check=True)

            pe.wait_ge(ys_ready, 1)
            pe.wait_ge(wsq_ready, 1)
            for m in range(KC):
                mm = product(z_rec_bank[:, m * B:(m + 1) * B], w_mod_sq, m, lambda k: ys_sq[:, k, :], m == 0)
            mm.then_inc(dsq_ready, 1)
            pe.wait_ge(ld_wmod, 16)
            for i in range(GROUPS):
                pe.wait_ge(xs_ready, i + 1)
                if i >= 2:
                    pe.wait_ge(lin_ready, i - 1)
                for m in range(KC):
                    mm = product(lin_bank[i % 2][m][:, :], w_mod, m,
                                 lambda k: xs[:, k, i * T // GROUPS:(i + 1) * T // GROUPS, :]
                                 .rearrange("p t b -> p (t b)"), True)
                mm.then_inc(linp_ready, 1)
                if i == 1:
                    pe.wait_ge(ld_win, 16)
                    pe.wait_ge(bias_ready, 1)
                    pe.wait_ge(x1_ready, 2)
                    for gate in (R, Z, G):
                        for m in range(KC):
                            for k in range(KC):
                                in_tile(0, 0, gate, m, k)
                            in_bias(0, gate, m)
            pe.wait_ge(lin_ready, GROUPS)
            pe.wait_ge(x1_ready, 1 + GROUPS)
            pe.wait_ge(part_ready, 2)
            pe.wait_ge(rest_ready, 2)
            pe.wait_ge(ld_wout, 16)

            OUT_AT = {1: (0, 0), 2: (0, 1), 3: (1, 0), 4: (1, 1)}
            IN_AT = {j: c for j, c in zip((0, 5, 6, 7, 8, 9, 10, 11, 12, 13, 14, 15),
                                          [(g, m, k) for g in (R, Z, G) for m in range(KC) for k in range(KC)])}

            FIRST_PART = ((0, 0), (1, 0), (0, 1), (1, 1))

            with pe.Fori(0, ITERS) as it:
                for s in range(BODY):
                    t = it * BODY + s
                    p, j = s // BLOCK, s % BLOCK
                    n = it * 2 + p
                    before = (s - 1) % BODY

                    for k, m in FIRST_PART:
                        if m == 0:
                            pe.wait_ge(h_ready[k], t + 1)
                        for wp in range(PARTS):
                            rec(pre(p, R, m, j, j + 1), R, m, k, wp, h_parts(k, before, 0, 1))
                    for k in range(KC):
                        pe.wait_ge(h_rest[k], t + 1)
                        for m in range(KC):
                            for wp in range(2):
                                rec(pre(p, R, m, j, j + 1), R, m, k, wp, h_parts(k, before, 1, 2))
                    pe.wait_ge(h_rest2, t + 1)
                    for m in range(KC):
                        for k in range(KC):
                            mm = rec(pre(p, R, m, j, j + 1), R, m, k, 0, h_parts(k, before, 2, 3))
                        mm.then_inc(pre_r[m], 1)

                    for m in range(KC):
                        for k in range(KC):
                            for wp in range(3):
                                mm = rec(z_rec_bank[:, m * PARTS * B:(m + 1) * PARTS * B], Z, m, k, wp,
                                         h_parts(k, before, 0, PARTS), m == 0 and k == 0 and wp == 0)
                    mm.then_inc(rec_z, 1)

                    for k, m in FIRST_PART:
                        if m == 0:
                            pe.wait_ge(rh_ready[k], t + 1)
                        for wp in range(PARTS):
                            rec(pre(p, G, m, j, j + 1), G, m, k, wp, rh_parts(k, 0, 1))
                    pe.wait_ge(rh_rest, t + 1)
                    for m in range(KC):
                        for k in range(KC):
                            for wp in range(2):
                                rec(pre(p, G, m, j, j + 1), G, m, k, wp, rh_parts(k, 1, 2))
                    pe.wait_ge(rh_rest2, t + 1)
                    for m in range(KC):
                        for k in range(KC):
                            mm = rec(pre(p, G, m, j, j + 1), G, m, k, 0, rh_parts(k, 2, 3))
                        mm.then_inc(pre_g[m], 1)

                    if j in OUT_AT:
                        m, k = OUT_AT[j]
                        if m == 0 and k == 0 and p == 1:
                            pe.wait_ge(res_ready, n * KC)
                        mm = out_tile(1 - p, m, k)
                        if m == KC - 1 and k == KC - 1:
                            mm.then_inc(y_ready, 1)
                    if j in IN_AT:
                        gate, m, k = IN_AT[j]
                        in_tile(n + 1, 1 - p, gate, m, k)
                        if k == KC - 1:
                            in_bias(1 - p, gate, m)

            for k in range(KC):
                pe.wait_ge(h_ready[k], T + 1)
            pe.wait_ge(res_ready, KC * NB)
            for m in range(KC):
                for k in range(KC):
                    mm = out_tile(1, m, k)
            mm.then_inc(y_ready, 1)


def kernel(**inputs):
    import numpy as np
    import concourse.bacc as bacc
    from concourse.bass_utils import run_bass_kernel_spmd

    def channel_major(a):
        return np.ascontiguousarray(np.asarray(a).T.reshape(-1, 128, a.shape[0]).transpose(1, 0, 2))

    x = np.asarray(inputs["x"])
    nb, nt, nch = x.shape
    w = {g: (inputs[f"L1_cond_Wx{g}"], inputs[f"L1_cond_Wh{g}"]) for g in "rzh"}
    bias = np.zeros((96, 3, nch), x.dtype)
    for i, g in enumerate("rzh"):
        for row in (0, 32, 64):
            bias[row, i] = inputs[f"L1_cond_bx{g}"]
            bias[row + 1, i] = inputs[f"L1_cond_bh{g}"]
    arrays = {
        "x_cm": channel_major(x.transpose(1, 0, 2).reshape(nt * nb, nch)),
        "cond_cm": channel_major(inputs["cond_1024"]),
        "w_mod_cm": channel_major(np.asarray(inputs["L0_cond_weight"]).T),
        "w_in_cm": np.ascontiguousarray(np.stack([channel_major(w[g][0]) for g in "rzh"], 1)),
        "w_rec_cm": np.ascontiguousarray(np.stack([channel_major(w[g][1]) for g in "rzh"], 1)),
        "w_out_cm": channel_major(inputs["L1_cond_Whq"]),
        "gate_bias": bias,
        "out_bias": np.ascontiguousarray(np.asarray(inputs["L1_cond_bhq"]).reshape(-1, 128).T),
    }
    nc = bacc.Bacc("TRN2", target_bir_lowering=False, num_devices=1)
    args = [nc.dram_tensor(k, a.shape, mybir.dt.from_np(a.dtype), kind="ExternalInput").ap() for k, a in arrays.items()]
    out = nc.dram_tensor("out_cm", (128, nch // 128, (nt + 16) * nb), mybir.dt.from_np(x.dtype), kind="ExternalOutput").ap()
    modulated_linear_then_gru(nc, *args, out)
    got = run_bass_kernel_spmd(nc, [arrays], core_ids=[0]).results[0]["out_cm"]
    return np.ascontiguousarray(got[:, :, 16 * nb:].reshape(128, nch // 128, nt, nb).transpose(3, 2, 1, 0).reshape(nb, nt, nch))
```

```python
import concourse.bass as bass
from concourse import mybir
from contextlib import ExitStack


def modulated_linear_then_gru(
    nc: bass.Bass,
    x_cm: bass.AP,
    cond_cm: bass.AP,
    w_mod_cm: bass.AP,
    w_in_cm: bass.AP,
    w_rec_cm: bass.AP,
    w_out_cm: bass.AP,
    gate_bias: bass.AP,
    z_bias: bass.AP,
    out_bias: bass.AP,
    out: bass.AP,
):
    fp32 = mybir.dt.float32
    bf16 = mybir.dt.bfloat16
    ALU = mybir.AluOpType
    ACT = mybir.ActivationFunctionType

    P = 128
    KC = x_cm.shape[1]
    C = P * KC
    B = cond_cm.shape[2]
    T = x_cm.shape[2] // B
    BLOCK = 16
    BC = BLOCK * B
    BODY = 4 * BLOCK
    ITERS = T // BODY
    SLOTS = 2 * BLOCK
    NB = T // BLOCK
    GROUPS = 4
    GC = T * B // GROUPS
    PARTS = 3
    Z_GROUPS = PARTS + 1
    R, Z, G = 0, 1, 2
    EPS = 1e-8
    SCALE = float(C) ** -0.5

    ctx = ExitStack()
    with ctx:
        def sb(name, shape, dt=fp32):
            return ctx.enter_context(nc.sbuf_tensor(name, shape, dt))

        def pb(name):
            return ctx.enter_context(nc.psum_tensor(name, [P, 512], fp32))

        def sem(name):
            return ctx.enter_context(nc.semaphore(name))

        x = sb("x", [P, KC, T * B])
        x1, x1_rest, x1_rest2 = (sb(name, [P, KC, (1 + NB + 1) * BC]) for name in ("x1", "x1_rest", "x1_rest2"))
        cond = sb("cond", [P, KC, B])
        w_mod = sb("w_mod", [P, KC, C])
        w_in, w_in_rest, w_in_rest2 = (sb(name, [P, 3, KC, C]) for name in ("w_in", "w_in_rest", "w_in_rest2"))
        w_out, w_out_rest, w_out_rest2 = (sb(name, [P, KC, C]) for name in ("w_out", "w_out_rest", "w_out_rest2"))
        w_rec = sb("w_rec", [P, 3, KC, C])
        w_rec_rest = sb("w_rec_rest", [P, 3, KC, C])
        w_part = [sb(f"w_part{i}", [P, 3, KC, C], bf16) for i in range(PARTS)]
        bq = sb("bq", [P, KC])

        bias_rows = sb("bias_rows", [96, 2, C])
        ones = sb("ones", [96, BC], bf16)
        z_bx_bh = sb("z_bx_bh", [P, 2, KC])
        bias_z = sb("bias_z", [P, KC])
        z_in = sb("z_in", [P, 2, KC, BLOCK, B])

        ys = sb("ys", [P, KC, B])
        ys_sq = sb("ys_sq", [P, KC, B])
        w_mod_sq = sb("w_mod_sq", [P, KC, C])
        d_sq = sb("d_sq", [P, KC, B])
        minus_half = sb("minus_half", [P, KC, B])
        d = sb("d", [P, KC, B])
        xs = sb("xs", [P, KC, T, B])
        lin = sb("lin", [P, KC, T, B])

        PART = 3 * B
        hidden = sb("hidden", [P, KC, SLOTS, PARTS * PART])
        r_hidden = sb("r_hidden", [P, KC, PARTS, B])
        z_pre = sb("z_pre", [P, KC, B])
        scan_mul = sb("scan_mul", [P, KC, PART])
        result = sb("result", [P, 2, KC, BC])

        def high(words):
            return words.bitcast(bf16).rearrange(
                {2: "p (c two) -> p c two", 3: "p k (c two) -> p k c two",
                 4: "p g k (c two) -> p g k c two"}[len(words.shape)], two=2)[..., 1]

        hidden_bf = hidden[:, :, :, :].bitcast(bf16)
        r_hidden_bf = r_hidden[:, :, :, :].rearrange("p k g b -> p k (g b)").bitcast(bf16)
        every_chunk = slice(0, KC)

        def h_word(k, slot, part=0):
            return hidden[:, k, slot, PART * part + 2:PART * (part + 1):3]

        def h_parts(k, slot, lo, hi):
            return hidden_bf[:, k, slot, 2 * PART * lo + 5:2 * PART * hi:6]

        def rh_parts(k, lo, hi):
            return r_hidden_bf[:, k, 2 * B * lo + 1:2 * B * hi:2]

        chunk_bank = [[pb(f"chunk_bank{p}{k}") for k in range(KC)] for p in range(2)]
        z_bank = pb("z_bank")
        z_rec_bank = pb("z_rec_bank")
        y_bank = pb("y_bank")
        r_bank = pb("r_bank")
        r_gate = [bank[:, KC * BC:KC * BC + B] for bank in (r_bank, z_bank)]
        lin_bank = [[r_bank, y_bank], chunk_bank[1]]

        def pre(parity, gate, m, lo, hi):
            if gate == Z:
                return z_bank[:, m * BC + lo * B:m * BC + hi * B]
            at = 0 if gate == R else BC
            return chunk_bank[parity][m][:, at + lo * B:at + hi * B]

        ld_cond, ld_wmod, ld_bias, ld_bq = sem("ld_cond"), sem("ld_wmod"), sem("ld_bias"), sem("ld_bq")
        ld_zbias = sem("ld_zbias")
        ld_x = [sem(f"ld_x{i}") for i in range(GROUPS)]
        ld_win, ld_wrec, ld_wout = sem("ld_win"), sem("ld_wrec"), sem("ld_wout")
        dve_step = sem("dve_step")
        ys_ready = sem("ys_ready")
        wsq_ready = sem("wsq_ready")
        dsq_ready = sem("dsq_ready")
        d_sq_ready = sem("d_sq_ready")
        exponent_ready = sem("exponent_ready")
        d_ready = sem("d_ready")
        bias_ready = sem("bias_ready")
        in0_ready = sem("in0_ready")
        part_ready = sem("part_ready")
        rest_ready = sem("rest_ready")
        bulk_rest = sem("bulk_rest")
        bulk_parts = sem("bulk_parts")
        x1_own = sem("x1_own")
        x1_parts = sem("x1_parts")
        z_ready = sem("z_ready")
        xs_ready = sem("xs_ready")
        linp_ready = sem("linp_ready")
        lin_ready = sem("lin_ready")
        x1_ready = sem("x1_ready")
        y_ready = sem("y_ready")
        res_ready = sem("res_ready")
        stored = [sem(f"stored{q}") for q in range(2)]
        pre_r = [sem(f"pre_r{k}") for k in range(KC)]
        z_seeded = sem("z_seeded")
        rec_z = sem("rec_z")
        pre_g = [sem(f"pre_g{k}") for k in range(KC)]
        r_ready = [sem(f"r_ready{k}") for k in range(KC)]
        g_ready = [sem(f"g_ready{k}") for k in range(KC)]
        rh_ready = [sem(f"rh_ready{k}") for k in range(KC)]
        rh_rest = [sem(f"rh_rest{k}") for k in range(KC)]
        rh_rest2 = [sem(f"rh_rest2{k}") for k in range(KC)]
        pre_z = sem("pre_z")
        h_ready = [sem(f"h_ready{k}") for k in range(KC)]
        h_rest = [sem(f"h_rest{k}") for k in range(KC)]
        h_rest2 = [sem(f"h_rest2{k}") for k in range(KC)]

        block = ctx.enter_context(nc.Block())

        @block.sync
        def _(sp):
            sp.dma_start(cond[:, :, :], cond_cm).then_inc(ld_cond, 16)
            for q in range(2):
                sp.sem_inc(stored[q], 16)
            for k in range(KC):
                sp.sem_inc(g_ready[k], 1)
            sp.dma_start(x[:, :, 0:GC], x_cm[:, :, 0:GC]).then_inc(ld_x[0], 16)
            sp.dma_start(w_rec[:, :, :, :], w_rec_cm).then_inc(ld_wrec, 16)
            for i in range(1, GROUPS):
                at = slice(i * GC, (i + 1) * GC)
                sp.dma_start(x[:, :, at], x_cm[:, :, at]).then_inc(ld_x[i], 16)
                if i == 1:
                    sp.dma_start(w_out[:, :, :], w_out_cm).then_inc(ld_wout, 16)
                if i == 2:
                    sp.dma_start(w_in[:, :, :, :], w_in_cm).then_inc(ld_win, 16)

            def store(n, parity):
                sp.wait_ge(res_ready, (n + 1) * KC)
                sp.dma_start(out[:, :, bass.ds(n * BC, BC)], result[:, 1 - parity, :, :]
                             ).then_inc(stored[1 - parity], 16)

            with sp.Fori(0, ITERS) as it:
                for b in range(BODY // BLOCK):
                    store(it * (BODY // BLOCK) + b, b % 2)
            store(NB, 0)
            sp.wait_ge(stored[0], 16 + 16 * (NB // 2))
            sp.wait_ge(stored[1], 16 + 16 * (NB // 2 + 1))

        @block.gpsimd
        def _(pool):
            nc.gpsimd.memset(minus_half[:, :, :], -0.5).then_inc(exponent_ready, 1)
            nc.gpsimd.memset(x1[:, :, 0:BC], 0.0)
            nc.gpsimd.memset(hidden[:, :, BLOCK:SLOTS - 1, 2::3], 0.0)
            nc.gpsimd.memset(x1[:, :, (1 + NB) * BC:], 0.0).then_inc(x1_ready, 1)
            pool.wait_ge(exponent_ready, 1)
            pool.wait_ge(d_sq_ready, 1)
            nc.gpsimd.tensor_tensor(d[:, :, :], d_sq[:, :, :], minus_half[:, :, :], ALU.pow).then_inc(d_ready, 1)

            def split_weight(w, rest, rest2, nth):
                nc.gpsimd.tensor_tensor(rest[...], w[...], high(w[...]), ALU.subtract).then_inc(bulk_rest, 1)
                pool.wait_ge(bulk_rest, nth)
                nc.gpsimd.tensor_tensor(rest2[...], rest[...], high(rest[...]), ALU.subtract).then_inc(bulk_parts, 1)

            for i in range(GROUPS):
                pool.wait_ge(lin_ready, i + 1)
                for k in range(KC):
                    add = nc.gpsimd.tensor_tensor(
                        x1[:, k, BC + i * GC:BC + (i + 1) * GC],
                        lin[:, k, :, :].rearrange("p t b -> p (t b)")[:, i * GC:(i + 1) * GC],
                        x[:, k, i * GC:(i + 1) * GC], ALU.add)
                add.then_inc(x1_ready, 1)
                if i == 0:
                    pool.wait_ge(ld_wout, 16)
                    split_weight(w_out, w_out_rest, w_out_rest2, 1)
                if i == 2:
                    pool.wait_ge(ld_win, 16)
                    split_weight(w_in, w_in_rest, w_in_rest2, 2)
            pool.wait_ge(x1_ready, 1 + GROUPS)
            with pool.Fori(0, NB) as n:
                cols = bass.ds((n + 2) * BC, BC)
                nc.gpsimd.tensor_tensor(x1_rest[:, :, cols], x1[:, :, cols], high(x1[:, :, :])[:, :, cols],
                                        ALU.subtract).then_inc(x1_own, 1)
                pool.wait_ge(x1_own, n + 1)
                nc.gpsimd.tensor_tensor(x1_rest2[:, :, cols], x1_rest[:, :, cols], high(x1_rest[:, :, :])[:, :, cols],
                                        ALU.subtract).then_inc(x1_parts, 1)

        @block.scalar
        def _(act):
            act.dma_start(w_mod[:, :, :], w_mod_cm).then_inc(ld_wmod, 16)
            act.dma_start(bias_rows[:, :, :], gate_bias).then_inc(ld_bias, 16)
            act.dma_start(z_bx_bh[:, :, :], z_bias).then_inc(ld_zbias, 16)
            act.dma_start(bq[:, :], out_bias).then_inc(ld_bq, 16)
            act.wait_ge(ld_wrec, 16)
            nc.scalar.activation(w_part[0][:, :, :, :], w_rec[:, :, :, :], ACT.Copy).then_inc(part_ready, 1)
            act.wait_ge(rest_ready, 1)
            nc.scalar.activation(w_part[1][:, :, :, :], w_rec_rest[:, :, :, :], ACT.Copy).then_inc(part_ready, 1)

            def seed_z(parity, j):
                nc.scalar.activation(
                    z_rec_bank[:, 0:KC * Z_GROUPS * B].rearrange("p (m g b) -> p m g b", m=KC, g=Z_GROUPS)[:, :, PARTS, :],
                    z_in[:, parity, :, j, :], ACT.Copy).then_inc(z_seeded, 1)

            act.wait_ge(z_seeded, 1)

            with act.Fori(0, ITERS) as it:
                for s in range(BODY):
                    t = it * BODY + s
                    p, j = s // BLOCK % 2, s % BLOCK
                    for k in range(KC):
                        act.wait_ge(pre_r[k], t + 1)
                        nc.scalar.activation(r_gate[k], pre(p, R, k, j, j + 1),
                                             ACT.Sigmoid).then_inc(r_ready[k], 1)
                    act.wait_ge(pre_z, t + 1)
                    nc.scalar.activation(scan_mul[:, :, 2::3], z_pre[:, :, :], ACT.Sigmoid, scale=-1.0)
                    for k in range(KC):
                        act.wait_ge(pre_g[k], t + 1)
                        nc.scalar.activation(hidden[:, k, (s - 1) % SLOTS, 3:3 + PART:3], pre(p, G, k, j, j + 1),
                                             ACT.Tanh).then_inc(g_ready[k], 1)
                    seed_z((s + 1) // BLOCK % 2, (s + 1) % BLOCK)

        @block.vector
        def _(dve):
            done = [0]

            def own(ins):
                done[0] += 1
                ins.then_inc(dve_step, 1)
                dve.wait_ge(dve_step, done[0])

            def split_h(slot, t1):
                for k in range(KC):
                    dve.wait_ge(h_ready[k], t1)
                    nc.vector.tensor_tensor(h_word(k, slot, 1), h_word(k, slot), h_parts(k, slot, 0, 1), ALU.subtract
                                            ).then_inc(h_rest[k], 1)
                for k in range(KC):
                    dve.wait_ge(h_rest[k], t1)
                    nc.vector.tensor_tensor(h_word(k, slot, 2), h_word(k, slot, 1), h_parts(k, slot, 1, 2), ALU.subtract
                                            ).then_inc(h_rest2[k], 1)
                nc.vector.tensor_copy(hidden[:, :, slot, 4:4 + PART:3], h_word(every_chunk, slot))

            dve.wait_ge(ld_cond, 16)
            own(nc.vector.tensor_scalar(ys[:, :, :], cond[:, :, :], SCALE, None, ALU.mult))
            nc.vector.tensor_tensor(ys_sq[:, :, :], ys[:, :, :], ys[:, :, :], ALU.mult).then_inc(ys_ready, 1)
            dve.wait_ge(ld_wmod, 16)
            nc.vector.tensor_tensor(w_mod_sq[:, :, :], w_mod[:, :, :], w_mod[:, :, :], ALU.mult).then_inc(wsq_ready, 1)

            def scale_x(i):
                dve.wait_ge(ld_x[i], 16)
                steps = slice(i * T // GROUPS, (i + 1) * T // GROUPS)
                for k in range(KC):
                    mul = nc.vector.tensor_tensor(
                        xs[:, k, steps, :], x[:, k, i * GC:(i + 1) * GC].rearrange("p (t b) -> p t b", b=B),
                        ys[:, k, :].unsqueeze(1).to_broadcast([P, T // GROUPS, B]), ALU.mult)
                mul.then_inc(xs_ready, 1)

            def modulate(i):
                dve.wait_ge(linp_ready, i + 1)
                steps = slice(i * T // GROUPS, (i + 1) * T // GROUPS)
                for k in range(KC):
                    mul = nc.vector.tensor_tensor(
                        lin[:, k, steps, :], lin_bank[i % 2][k][:, :].rearrange("p (t b) -> p t b", b=B),
                        d[:, k, :].unsqueeze(1).to_broadcast([P, T // GROUPS, B]), ALU.mult)
                mul.then_inc(lin_ready, 1)

            def take_z(parity, m):
                nc.vector.tensor_scalar(z_in[:, parity, m, :, :].rearrange("p s b -> p (s b)"),
                                        z_bank[:, m * BC:(m + 1) * BC], bias_z[:, m:m + 1], None, ALU.add)

            scale_x(0)
            dve.wait_ge(dsq_ready, 1)
            nc.vector.tensor_scalar(d_sq[:, :, :], z_rec_bank[:, 0:KC * B].rearrange("p (k b) -> p k b", k=KC),
                                    EPS, None, ALU.add).then_inc(d_sq_ready, 1)
            for k in range(KC):
                nc.vector.tensor_copy(h_word(k, SLOTS - 1), cond[:, k, :]).then_inc(h_ready[k], 1)
            split_h(SLOTS - 1, 1)
            nc.vector.memset(scan_mul[:, :, 0::3], 0.0)
            nc.vector.memset(scan_mul[:, :, 1::3], -1.0)
            nc.vector.memset(ones[:, :], 1.0)
            scale_x(1)
            dve.wait_ge(part_ready, 1)
            nc.vector.tensor_tensor(w_rec_rest[:, :, :, :], w_rec[:, :, :, :], w_part[0][:, :, :, :],
                                    ALU.subtract).then_inc(rest_ready, 1)
            dve.wait_ge(d_ready, 1)
            modulate(0)
            scale_x(2)
            dve.wait_ge(ld_bias, 16)
            for group in (64, 32):
                rows = bias_rows[group:group + 32, :, :]
                own(nc.vector.tensor_tensor(rows, rows, high(rows), ALU.subtract))
            modulate(1)
            scale_x(3)
            rows = bias_rows[64:96, :, :]
            nc.vector.tensor_tensor(rows, rows, high(rows), ALU.subtract).then_inc(bias_ready, 1)
            dve.wait_ge(part_ready, 2)
            nc.vector.tensor_tensor(w_part[2][:, :, :, :], w_rec_rest[:, :, :, :], w_part[1][:, :, :, :],
                                    ALU.subtract).then_inc(rest_ready, 1)
            modulate(2)
            dve.wait_ge(ld_zbias, 16)
            own(nc.vector.tensor_tensor(bias_z[:, :], z_bx_bh[:, 0, :], z_bx_bh[:, 1, :], ALU.add))
            modulate(3)
            dve.wait_ge(in0_ready, 1)
            for m in range(KC):
                take_z(0, m)
            for m in range(KC):
                at = (m * Z_GROUPS + PARTS) * B
                seed = nc.vector.tensor_scalar(z_rec_bank[:, at:at + B], z_bank[:, m * BC:m * BC + B],
                                               bias_z[:, m:m + 1], None, ALU.add)
            seed.then_inc(z_seeded, 1)
            dve.wait_ge(ld_bq, 16)

            def finish(n, parity, k, slot_free):
                if k == 0:
                    dve.wait_ge(stored[1 - parity], slot_free)
                nc.vector.scalar_tensor_tensor(
                    out=result[:, 1 - parity, k, :], in0=y_bank[:, k * BC:(k + 1) * BC], scalar=bq[:, k:k + 1],
                    in1=x1[:, k, bass.ds(n * BC, BC)], op0=ALU.add, op1=ALU.add).then_inc(res_ready, 1)

            with dve.Fori(0, ITERS) as it:
                for s in range(BODY):
                    t = it * BODY + s
                    p, j = s // BLOCK % 2, s % BLOCK
                    n = it * (BODY // BLOCK) + s // BLOCK
                    before = (s - 1) % SLOTS
                    for k in range(KC):
                        dve.wait_ge(r_ready[k], t + 1)
                        nc.vector.tensor_tensor(r_hidden[:, k, 0, :], r_gate[k], h_word(k, before),
                                                ALU.mult).then_inc(rh_ready[k], 1)
                    for k in range(KC):
                        dve.wait_ge(rh_ready[k], t + 1)
                        nc.vector.tensor_tensor(r_hidden[:, k, 1, :], r_hidden[:, k, 0, :], rh_parts(k, 0, 1),
                                                ALU.subtract).then_inc(rh_rest[k], 1)
                    for k in range(KC):
                        dve.wait_ge(rh_rest[k], t + 1)
                        nc.vector.tensor_tensor(r_hidden[:, k, 2, :], r_hidden[:, k, 1, :], rh_parts(k, 1, 2),
                                                ALU.subtract).then_inc(rh_rest2[k], 1)
                    dve.wait_ge(rec_z, t + 1)
                    nc.vector.tensor_reduce(
                        z_pre[:, :, :], z_rec_bank[:, 0:KC * Z_GROUPS * B].rearrange(
                            "p (m g b) -> p m b g", m=KC, g=Z_GROUPS),
                        axis=mybir.AxisListType.X, op=ALU.add).then_inc(pre_z, 1)
                    if j in (4, 5):
                        if j == 4:
                            dve.wait_ge(y_ready, n + 1)
                        finish(n, p, j - 4, it * (16 * BODY // SLOTS) + 16 * (s // SLOTS) + 16)
                    if j in (10, 11):
                        if j == 10:
                            dve.wait_ge(z_ready, n + 1)
                        take_z(1 - p, j - 10)
                    for k in range(KC):
                        dve.wait_ge(g_ready[k], t + 2)
                        nc.vector.tensor_tensor_scan(hidden[:, k, s % SLOTS, 0:PART], scan_mul[:, k, :],
                                                     hidden[:, k, before, 2:2 + PART], 0.0, ALU.mult, ALU.add
                                                     ).then_inc(h_ready[k], 1)
                    split_h(s % SLOTS, t + 2)

            dve.wait_ge(y_ready, NB + 1)
            for k in range(KC):
                finish(NB, 0, k, 16 + 16 * (NB // 2))

        @block.tensor
        def _(pe):
            def product(cols, w, m, moving, first):
                for k in range(KC):
                    mm = nc.tensor.matmul(cols, w[:, k, m * P:(m + 1) * P], moving(k),
                                          start=(first and k == 0), stop=True, skip_group_check=True)
                return mm

            def in_tile(n, parity, gate, m, k):
                first = k == 0 and (gate == R or (gate == Z and m == 0))
                return nc.tensor.matmul(pre(parity, gate, m, 0, BLOCK), w_in[:, gate, k, m * P:(m + 1) * P],
                                        x1[:, k, bass.ds((n + 1) * BC, BC)],
                                        start=first, stop=True, skip_group_check=True)

            def out_tile(parity, m, k):
                return nc.tensor.matmul(y_bank[:, m * BC:(m + 1) * BC], w_out[:, k, m * P:(m + 1) * P],
                                        h_word(k, slice(parity * BLOCK, (parity + 1) * BLOCK)),
                                        start=(m == 0 and k == 0), stop=True, skip_group_check=True)

            PRODUCTS = ((0, 0), (1, 0), (2, 0), (0, 1), (1, 1), (0, 2))
            W_IN = [high(w[:, :, :, :]) for w in (w_in, w_in_rest, w_in_rest2)]
            X1 = [high(x[:, :, :]) for x in (x1, x1_rest, x1_rest2)]
            W_OUT = [high(w[:, :, :]) for w in (w_out, w_out_rest, w_out_rest2)]

            def in_bias(parity, gate, m, steps):
                return nc.tensor.matmul(pre(parity, gate, m, steps.start, steps.stop),
                                        high(bias_rows[:, :, :])[:, gate // 2, m * P:(m + 1) * P],
                                        ones[:, 0:(steps.stop - steps.start) * B], start=False, stop=True,
                                        skip_group_check=True)

            def bulk_tiles(what, gate):
                return [(what, gate, m, k, i) for m in range(KC) for k in range(KC) for i in range(len(PRODUCTS))]

            outs, z_tiles, others = bulk_tiles("out", None), bulk_tiles("in", Z), bulk_tiles("in", R) + bulk_tiles("in", G)
            BULK = []
            for j in range(BLOCK):
                for i in range(6):
                    BULK.append((outs or (i > 0 and z_tiles) or others).pop(0))

            HALVES = (slice(0, BLOCK // 2), slice(BLOCK // 2, BLOCK))
            BIAS_AT = dict(zip(range(BLOCK - 8, BLOCK), [(gate, m, half) for m in range(KC) for gate in (R, G)
                                                         for half in HALVES]))

            def bulk(at, n, p):
                what, gate, m, k, i = BULK[at]
                wp, part = PRODUCTS[i]
                cols = slice(m * P, (m + 1) * P)
                first = k == 0 and i == 0
                last = k == KC - 1 and m == KC - 1 and i == 5
                if what == "out":
                    if at == 0:
                        pe.wait_ge(bulk_parts, 1)
                    mm = nc.tensor.matmul(y_bank[:, m * BC:(m + 1) * BC], W_OUT[wp][:, k, cols],
                                          h_parts(k, slice((1 - p) * BLOCK, (2 - p) * BLOCK), part, part + 1),
                                          start=(first and m == 0), stop=True, skip_group_check=True)
                    if last:
                        mm.then_inc(y_ready, 1)
                else:
                    if gate == R and first and m == 0:
                        pe.wait_ge(x1_parts, n + 1)
                    mm = nc.tensor.matmul(pre(1 - p, gate, m, 0, BLOCK), W_IN[wp][:, gate, k, cols],
                                          X1[part][:, k, bass.ds((n + 2) * BC, BC)],
                                          start=first and (gate == R or (gate == Z and m == 0)),
                                          stop=True, skip_group_check=True)
                    if gate == Z and last:
                        mm.then_inc(z_ready, 1)

            def rec(cols, gate, m, k, wp, moving, first=False):
                return nc.tensor.matmul(cols, w_part[wp][:, gate, k, m * P:(m + 1) * P], moving,
                                        start=first, stop=True, skip_group_check=True)

            pe.wait_ge(ys_ready, 1)
            pe.wait_ge(wsq_ready, 1)
            for m in range(KC):
                mm = product(z_rec_bank[:, m * B:(m + 1) * B], w_mod_sq, m, lambda k: ys_sq[:, k, :], m == 0)
            mm.then_inc(dsq_ready, 1)
            pe.wait_ge(ld_wmod, 16)
            for i in range(GROUPS):
                pe.wait_ge(xs_ready, i + 1)
                if i >= 2:
                    pe.wait_ge(lin_ready, i - 1)
                for m in range(KC):
                    mm = product(lin_bank[i % 2][m][:, :], w_mod, m,
                                 lambda k: xs[:, k, i * T // GROUPS:(i + 1) * T // GROUPS, :]
                                 .rearrange("p t b -> p (t b)"), True)
                mm.then_inc(linp_ready, 1)
            pe.wait_ge(ld_win, 16)
            pe.wait_ge(lin_ready, 3)
            pe.wait_ge(x1_ready, 2)
            for gate in (Z, R, G):
                if gate == R:
                    pe.wait_ge(bias_ready, 1)
                for m in range(KC):
                    for k in range(KC):
                        mm = in_tile(0, 0, gate, m, k)
                    if gate != Z:
                        in_bias(0, gate, m, slice(0, BLOCK))
                if gate == Z:
                    mm.then_inc(in0_ready, 1)
            pe.wait_ge(rest_ready, 2)

            def gate_products(gate, t, p, j, parts, ready, bank1_read, rest, rest2, done):
                def products(m, k, w_parts, part):
                    for wp in range(w_parts):
                        mm = rec(pre(p, gate, m, j, j + 1), gate, m, k, wp, parts(k, part, part + 1))
                    return mm

                pe.wait_ge(ready[0], t + 1)
                products(0, 0, 3, 0)
                pe.wait_ge(bank1_read, t + 1)
                products(1, 0, 3, 0)
                pe.wait_ge(ready[1], t + 1)
                products(0, 1, 3, 0)
                products(1, 1, 3, 0)
                for k in range(KC):
                    pe.wait_ge(rest[k], t + 1)
                    products(0, k, 2, 1)
                pe.wait_ge(rest2[0], t + 1)
                products(0, 0, 1, 2)
                products(1, 0, 2, 1)
                pe.wait_ge(rest2[1], t + 1)
                products(0, 1, 1, 2).then_inc(done[0], 1)
                products(1, 1, 2, 1)
                products(1, 0, 1, 2)
                products(1, 1, 1, 2).then_inc(done[1], 1)

            with pe.Fori(0, ITERS) as it:
                for s in range(BODY):
                    t = it * BODY + s
                    p, j = s // BLOCK % 2, s % BLOCK
                    n = it * (BODY // BLOCK) + s // BLOCK
                    before = (s - 1) % SLOTS

                    gate_products(R, t, p, j, lambda k, lo, hi: h_parts(k, before, lo, hi),
                                  h_ready, g_ready[1], h_rest, h_rest2, pre_r)
                    pe.wait_ge(z_seeded, t + 1)
                    for m in range(KC):
                        for k in range(KC):
                            for wp in range(PARTS):
                                mm = rec(z_rec_bank[:, m * Z_GROUPS * B:(m * Z_GROUPS + PARTS) * B], Z, m, k, wp,
                                         h_parts(k, before, 0, PARTS), m == 0 and k == 0 and wp == 0)
                    mm.then_inc(rec_z, 1)

                    bulk(6 * j, n, p)
                    if j in BIAS_AT:
                        in_bias(1 - p, *BIAS_AT[j])

                    gate_products(G, t, p, j, rh_parts, rh_ready, r_ready[1], rh_rest, rh_rest2, pre_g)

                    for i in range(1, 6):
                        bulk(6 * j + i, n, p)

            for k in range(KC):
                pe.wait_ge(h_ready[k], T + 1)
            pe.wait_ge(res_ready, KC * NB)
            for m in range(KC):
                for k in range(KC):
                    mm = out_tile(1, m, k)
            mm.then_inc(y_ready, 1)


def kernel(**inputs):
    import numpy as np
    import concourse.bacc as bacc
    from concourse.bass_utils import run_bass_kernel_spmd

    def channel_major(a):
        return np.ascontiguousarray(np.asarray(a).T.reshape(-1, 128, a.shape[0]).transpose(1, 0, 2))

    x = np.asarray(inputs["x"])
    nb, nt, nch = x.shape
    w = {g: (inputs[f"L1_cond_Wx{g}"], inputs[f"L1_cond_Wh{g}"]) for g in "rzh"}
    gate_bias = np.zeros((96, 2, nch), x.dtype)
    for i, g in enumerate("rh"):
        for row in (0, 32, 64):
            gate_bias[row, i] = inputs[f"L1_cond_bx{g}"]
            gate_bias[row + 1, i] = inputs[f"L1_cond_bh{g}"]
    arrays = {
        "x_cm": channel_major(x.transpose(1, 0, 2).reshape(nt * nb, nch)),
        "cond_cm": channel_major(inputs["cond_1024"]),
        "w_mod_cm": channel_major(np.asarray(inputs["L0_cond_weight"]).T),
        "w_in_cm": np.ascontiguousarray(np.stack([channel_major(w[g][0]) for g in "rzh"], 1)),
        "w_rec_cm": np.ascontiguousarray(np.stack([channel_major(w[g][1]) for g in "rzh"], 1)),
        "w_out_cm": channel_major(inputs["L1_cond_Whq"]),
        "gate_bias": gate_bias,
        "z_bias": np.ascontiguousarray(np.stack(
            [inputs[f"L1_cond_b{a}z"].reshape(-1, 128).T for a in "xh"], 1)),
        "out_bias": np.ascontiguousarray(np.asarray(inputs["L1_cond_bhq"]).reshape(-1, 128).T),
    }
    nc = bacc.Bacc("TRN2", target_bir_lowering=False, num_devices=1)
    args = [nc.dram_tensor(k, a.shape, mybir.dt.from_np(a.dtype), kind="ExternalInput").ap() for k, a in arrays.items()]
    out = nc.dram_tensor("out_cm", (128, nch // 128, (nt + 16) * nb), mybir.dt.from_np(x.dtype), kind="ExternalOutput").ap()
    modulated_linear_then_gru(nc, *args, out)
    got = run_bass_kernel_spmd(nc, [arrays], core_ids=[0]).results[0]["out_cm"]
    return np.ascontiguousarray(got[:, :, 16 * nb:].reshape(128, nch // 128, nt, nb).transpose(3, 2, 1, 0).reshape(nb, nt, nch))
```
